# Optimizing a Trainium2 kernel written in Bass

```python
import numpy as np
import jax
import jax.numpy as jnp

def _softmax(x, axis=-1):
    return jax.nn.softmax(x, axis=axis)

def _gelu(x):
    return jax.nn.gelu(x, approximate=True)

def _silu(x):
    return jax.nn.silu(x)

def _sigmoid(x):
    return jax.nn.sigmoid(x)

def _layernorm(x, axis=-1, eps=1e-05):
    m = jnp.mean(x, axis=axis, keepdims=True)
    v = jnp.var(x, axis=axis, keepdims=True)
    return (x - m) / jnp.sqrt(v + eps)

def _scatter_add(tgt, idx, src, axis=0):
    return tgt.at[idx].add(src)

def _segment_sum(src, seg, n):
    return jax.ops.segment_sum(src, seg, n)
kernel_name = 'mk_flamingo_gated_d2_seqx_r8_e27eec'

def setup_inputs(seed: int=0):
    np.random.seed(seed)
    _w = jnp.asarray

    def _rec_inputs():
        import jax
        import jax.numpy as jnp
        _rk = jax.random.key(seed)
        x = 7.22e-05 + 1 * jax.random.normal(jax.random.fold_in(_rk, 1), (16, 128, 128), jnp.float32)
        _lenS = 128 - jax.random.randint(jax.random.fold_in(_rk, 7), (16,), 0, max(1, 128 // 4) + 1, jnp.int32)
        _lenS2 = 77 - jax.random.randint(jax.random.fold_in(_rk, 8), (16,), 0, max(1, 77 // 4) + 1, jnp.int32)
        _ctx_1024P = jax.random.normal(jax.random.fold_in(_rk, 11), (16, 16, 128), jnp.float32)
        _ctx_1024c = jax.random.dirichlet(jax.random.fold_in(_rk, 511), 0.3 * jnp.ones((16,), jnp.float32), (16, 77))
        _ctx_1024t = jnp.einsum('bsk,bkd->bsd', _ctx_1024c, _ctx_1024P)
        _ctx_1024t = _ctx_1024t * jax.lax.rsqrt(jnp.mean(jnp.square(_ctx_1024t)) + 1e-12) * 0.953939
        ctx_1024 = 4.13588e-05 + 0.999923 * (_ctx_1024t + 0.3 * jax.random.normal(jax.random.fold_in(_rk, 611), (16, 77, 128), jnp.float32))
        _validS = jnp.arange(128)[None, :] < _lenS[:, None]
        _validS2 = jnp.arange(77)[None, :] < _lenS2[:, None]
        _causal = jnp.tril(jnp.ones((128, 128), dtype=bool))
        mask_BxS2_bf1 = jnp.ones((16, 77), dtype=bool)
        _g = jax.random.normal(jax.random.fold_in(_rk, 9001), (2, 2), jnp.float32)
        _g = jnp.sign(_g) * jnp.maximum(jnp.abs(_g), 1.0) + (_g == 0) * 1.0
        g_xattn = _g[0]
        g_ffn = _g[1]
        return (x, ctx_1024, mask_BxS2_bf1, g_xattn, g_ffn)
    x, ctx_1024, mask_BxS2_bf1, g_xattn, g_ffn = _rec_inputs()

    def _L0_xattn_setup():
        import jax, jax.numpy as jnp
        import numpy as np
        key = jax.random.key(seed)
        ks = jax.random.split(key, 7)
        B, S, D, H, Dh = (4, 256, 128, 16, 64)
        return {'query_input': jax.random.normal(ks[0], (B, S, D), jnp.float32), 'key_input': jax.random.normal(ks[1], (B, S, D), jnp.float32), 'value_input': jax.random.normal(ks[2], (B, S, D), jnp.float32), 'Wq': jax.random.normal(ks[3], (D, H, Dh), jnp.float32) * 0.03, 'Wk': jax.random.normal(ks[4], (D, H, Dh), jnp.float32) * 0.03, 'Wv': jax.random.normal(ks[5], (D, H, Dh), jnp.float32) * 0.03, 'Wo': jax.random.normal(ks[6], (H, Dh, D), jnp.float32) * 0.03}
    _L0_xattn_all = _L0_xattn_setup()
    _L0_xattn_in = {k: v for k, v in _L0_xattn_all.items() if k in ('Wq', 'Wk', 'Wv', 'Wo')}
    del _L0_xattn_all

    def _L0_ffn_setup():
        import jax, jax.numpy as jnp
        import numpy as np
        N_EXP = 8
        TOP_K = 2
        CAPACITY_FACTOR = 1.25
        key = jax.random.key(seed)
        ks = jax.random.split(key, 5)
        B, T, D = (4, 128, 128)
        H = 4 * D
        E = N_EXP
        x = jax.random.normal(ks[0], (B, T, D), jnp.float32)
        gate_w = jax.random.normal(ks[1], (D, E), jnp.float32) * 0.02
        c_fc = jax.random.normal(ks[2], (E, D, H), jnp.float32) * 0.02
        fc_bias = jnp.zeros((E, 1, H), jnp.float32)
        c_proj = jax.random.normal(ks[3], (E, H, D), jnp.float32) * 0.02
        proj_bias = jnp.zeros((E, 1, D), jnp.float32)
        return dict(x=x, gate_w=gate_w, c_fc=c_fc, fc_bias=fc_bias, c_proj=c_proj, proj_bias=proj_bias)
    _L0_ffn_all = _L0_ffn_setup()
    _L0_ffn_in = {k: v for k, v in _L0_ffn_all.items() if k in ('gate_w', 'c_fc', 'fc_bias', 'c_proj', 'proj_bias')}
    del _L0_ffn_all

    def _L1_xattn_setup():
        import jax, jax.numpy as jnp
        import numpy as np
        D_MODEL = 128
        N_HEADS = 16
        HEAD_DIM = D_MODEL // N_HEADS
        key = jax.random.key(seed)
        ks = jax.random.split(key, 11)
        B, Q, K = (4, 256, 256)
        s = 1.0 / np.sqrt(D_MODEL)
        inp = {'q': jax.random.normal(ks[0], (B, Q, D_MODEL), jnp.float32), 'k': jax.random.normal(ks[1], (B, K, D_MODEL), jnp.float32), 'v': jax.random.normal(ks[2], (B, K, D_MODEL), jnp.float32), 'kv_mask': jnp.ones((B, K), dtype=bool), 'Wq': jax.random.normal(ks[3], (D_MODEL, D_MODEL), jnp.float32) * s, 'bq': jnp.zeros((D_MODEL,), jnp.float32), 'Wk': jax.random.normal(ks[4], (D_MODEL, D_MODEL), jnp.float32) * s, 'bk': jnp.zeros((D_MODEL,), jnp.float32), 'Wv': jax.random.normal(ks[5], (D_MODEL, D_MODEL), jnp.float32) * s, 'bv': jnp.zeros((D_MODEL,), jnp.float32), 'Wo': jax.random.normal(ks[6], (D_MODEL, D_MODEL), jnp.float32) * s, 'bo': jnp.zeros((D_MODEL,), jnp.float32)}
        return inp
    _L1_xattn_all = _L1_xattn_setup()
    _L1_xattn_in = {k: v for k, v in _L1_xattn_all.items() if k in ('Wq', 'bq', 'Wk', 'bk', 'Wv', 'bv', 'Wo', 'bo')}
    del _L1_xattn_all

    def _L1_ffn_setup():
        import jax, jax.numpy as jnp
        import numpy as np
        B, S, D = (4, 512, 128)
        E, F_EXP = (16, 256)
        F_C = 2.0
        F_SH = 256
        key = jax.random.key(seed)
        ks = jax.random.split(key, 8)
        s = 0.02
        return {'hidden_states': jax.random.normal(ks[0], (B, S, D), jnp.float32), 'gate_w': jax.random.normal(ks[1], (E, D), jnp.float32) * s, 'Wg': jax.random.normal(ks[2], (E, F_EXP, D), jnp.float32) * s, 'Wu': jax.random.normal(ks[3], (E, F_EXP, D), jnp.float32) * s, 'Wd': jax.random.normal(ks[4], (E, D, F_EXP), jnp.float32) * s, 'Ws_g': jax.random.normal(ks[5], (F_SH, D), jnp.float32) * s, 'Ws_u': jax.random.normal(ks[6], (F_SH, D), jnp.float32) * s, 'Ws_d': jax.random.normal(ks[7], (D, F_SH), jnp.float32) * s}
    _L1_ffn_all = _L1_ffn_setup()
    _L1_ffn_in = {k: v for k, v in _L1_ffn_all.items() if k in ('gate_w', 'Wg', 'Wu', 'Wd', 'Ws_g', 'Ws_u', 'Ws_d')}
    del _L1_ffn_all
    return {'x': x, 'ctx_1024': ctx_1024, 'mask_BxS2_bf1': mask_BxS2_bf1, 'g_xattn': g_xattn, 'g_ffn': g_ffn, 'L0_xattn_Wq': _L0_xattn_in['Wq'], 'L0_xattn_Wk': _L0_xattn_in['Wk'], 'L0_xattn_Wv': _L0_xattn_in['Wv'], 'L0_xattn_Wo': _L0_xattn_in['Wo'], 'L0_ffn_gate_w': _L0_ffn_in['gate_w'], 'L0_ffn_c_fc': _L0_ffn_in['c_fc'], 'L0_ffn_fc_bias': _L0_ffn_in['fc_bias'], 'L0_ffn_c_proj': _L0_ffn_in['c_proj'], 'L0_ffn_proj_bias': _L0_ffn_in['proj_bias'], 'L1_xattn_Wq': _L1_xattn_in['Wq'], 'L1_xattn_bq': _L1_xattn_in['bq'], 'L1_xattn_Wk': _L1_xattn_in['Wk'], 'L1_xattn_bk': _L1_xattn_in['bk'], 'L1_xattn_Wv': _L1_xattn_in['Wv'], 'L1_xattn_bv': _L1_xattn_in['bv'], 'L1_xattn_Wo': _L1_xattn_in['Wo'], 'L1_xattn_bo': _L1_xattn_in['bo'], 'L1_ffn_gate_w': _L1_ffn_in['gate_w'], 'L1_ffn_Wg': _L1_ffn_in['Wg'], 'L1_ffn_Wu': _L1_ffn_in['Wu'], 'L1_ffn_Wd': _L1_ffn_in['Wd'], 'L1_ffn_Ws_g': _L1_ffn_in['Ws_g'], 'L1_ffn_Ws_u': _L1_ffn_in['Ws_u'], 'L1_ffn_Ws_d': _L1_ffn_in['Ws_d']}

def reference(x, ctx_1024, mask_BxS2_bf1, g_xattn, g_ffn, L0_xattn_Wq, L0_xattn_Wk, L0_xattn_Wv, L0_xattn_Wo, L0_ffn_gate_w, L0_ffn_c_fc, L0_ffn_fc_bias, L0_ffn_c_proj, L0_ffn_proj_bias, L1_xattn_Wq, L1_xattn_bq, L1_xattn_Wk, L1_xattn_bk, L1_xattn_Wv, L1_xattn_bv, L1_xattn_Wo, L1_xattn_bo, L1_ffn_gate_w, L1_ffn_Wg, L1_ffn_Wu, L1_ffn_Wd, L1_ffn_Ws_g, L1_ffn_Ws_u, L1_ffn_Ws_d):
    import jax
    import jax.numpy as jnp

    def _L0_xattn_ref(query_input, key_input, value_input, Wq, Wk, Wv, Wo):
        import jax, jax.numpy as jnp
        import numpy as np
        q = jnp.einsum('bsd,dhk->bshk', query_input, Wq)
        k = jnp.einsum('bsd,dhk->bshk', key_input, Wk)
        v = jnp.einsum('bsd,dhk->bshk', value_input, Wv)
        depth = Wq.shape[-1]
        q = q * depth ** (-0.5)
        logits = jnp.einsum('bthk,bfhk->bhft', k, q)
        weights = jax.nn.softmax(logits, axis=-1)
        ctx = jnp.einsum('bhft,bthk->bfhk', weights, v)
        return jnp.einsum('bfhk,hkd->bfd', ctx, Wo)

    def _L0_ffn_ref(x, gate_w, c_fc, fc_bias, c_proj, proj_bias):
        import jax, jax.numpy as jnp
        import numpy as np
        N_EXP = 8
        TOP_K = 2
        CAPACITY_FACTOR = 1.25
        B, T, D = x.shape
        n = B * T
        E, k = (N_EXP, TOP_K)
        cap = int(CAPACITY_FACTOR * n * k / E)
        xt = x.reshape(n, D)
        logits = xt @ gate_w
        top_logits, top_idx = jax.lax.top_k(logits, k)
        masked = jnp.full_like(logits, -jnp.inf)
        masked = masked.at[jnp.arange(n)[:, None], top_idx].set(top_logits)
        router_probs = jax.nn.softmax(masked, axis=-1)
        exp_mask = jax.nn.one_hot(top_idx, E, dtype=jnp.int32)
        exp_mask = jnp.transpose(exp_mask, (1, 0, 2))
        exp_rank = jnp.cumsum(exp_mask.reshape(k * n, E), axis=0) - 1
        exp_rank = exp_rank.reshape(k, n, E)
        exp_mask = exp_mask * (exp_rank < cap).astype(jnp.int32)
        used_capacity = jnp.sum(exp_mask, axis=(0, 1))
        exp_rank = jnp.sum(exp_mask * exp_rank, axis=-1)
        exp_weights = exp_mask.astype(x.dtype) * router_probs[None]
        rank_oh = jax.nn.one_hot(exp_rank, cap, dtype=x.dtype)
        cb_weight = jnp.einsum('kne,knc->nec', exp_weights, rank_oh)
        sec_mask = (cb_weight != 0).astype(x.dtype)
        exp_batches = jnp.einsum('nec,nd->ecd', sec_mask, xt)
        h = jnp.einsum('ecd,edh->ech', exp_batches, c_fc) + fc_bias
        h = jax.nn.gelu(h, approximate=False)
        exp_out = jnp.einsum('ech,ehd->ecd', h, c_proj) + proj_bias
        out = jnp.einsum('nec,ecd->nd', cb_weight, exp_out)
        return out.reshape(B, T, D)

    def _L1_xattn_ref(q, k, v, kv_mask, Wq, bq, Wk, bk, Wv, bv, Wo, bo):
        import jax, jax.numpy as jnp
        import numpy as np
        D_MODEL = 128
        N_HEADS = 16
        HEAD_DIM = D_MODEL // N_HEADS
        B, Qlen, _ = q.shape
        Klen = k.shape[1]
        qh = (q @ Wq.T + bq).reshape(B, Qlen, N_HEADS, HEAD_DIM).transpose(0, 2, 1, 3)
        kh = (k @ Wk.T + bk).reshape(B, Klen, N_HEADS, HEAD_DIM).transpose(0, 2, 1, 3)
        vh = (v @ Wv.T + bv).reshape(B, Klen, N_HEADS, HEAD_DIM).transpose(0, 2, 1, 3)
        score = jnp.einsum('bhqd,bhkd->bhqk', qh, kh) / np.sqrt(HEAD_DIM).astype(np.float32)
        score = jnp.where(kv_mask[:, None, None, :], score, jnp.float32(-10000.0))
        attn = jax.nn.softmax(score, axis=-1)
        out = jnp.einsum('bhqk,bhkd->bhqd', attn, vh)
        out = out.transpose(0, 2, 1, 3).reshape(B, Qlen, D_MODEL)
        return out @ Wo.T + bo

    def _L1_ffn_ref(hidden_states, gate_w, Wg, Wu, Wd, Ws_g, Ws_u, Ws_d):
        import jax, jax.numpy as jnp
        import numpy as np
        B, S, D = (4, 512, 128)
        E, F_EXP = (16, 256)
        F_C = 2.0
        F_SH = 256
        b, s, d = hidden_states.shape
        e = gate_w.shape[0]
        cap = int(s * F_C / e)
        logits = jnp.einsum('bsd,ed->bse', hidden_states, gate_w)
        scores = jax.nn.softmax(logits, axis=-1).transpose(0, 2, 1)
        topk_w, topk_idx = jax.lax.top_k(scores, cap)
        x_tok = jnp.take_along_axis(hidden_states[:, None, :, :], topk_idx[..., None], axis=2)
        g = jnp.einsum('becd,efd->becf', x_tok, Wg)
        u = jnp.einsum('becd,efd->becf', x_tok, Wu)
        h = jax.nn.gelu(g, approximate=False) * u
        eo = jnp.einsum('becf,edf->becd', h, Wd) * topk_w[..., None]
        offs = (jnp.arange(b) * s)[:, None, None]
        flat_idx = (topk_idx + offs).reshape(-1)
        flat = jnp.zeros((b * s, d), hidden_states.dtype)
        flat = flat.at[flat_idx].add(eo.reshape(-1, d))
        out = flat.reshape(b, s, d)
        gs = jnp.einsum('bsd,fd->bsf', hidden_states, Ws_g)
        us = jnp.einsum('bsd,fd->bsf', hidden_states, Ws_u)
        shared = jnp.einsum('bsf,df->bsd', jax.nn.gelu(gs, approximate=False) * us, Ws_d)
        return out + shared
    x = x + jnp.tanh(g_xattn[0]) * _L0_xattn_ref(_layernorm(x, axis=-1), ctx_1024, ctx_1024, L0_xattn_Wq, L0_xattn_Wk, L0_xattn_Wv, L0_xattn_Wo)
    x = x + jnp.tanh(g_ffn[0]) * _L0_ffn_ref(_layernorm(x, axis=-1), L0_ffn_gate_w, L0_ffn_c_fc, L0_ffn_fc_bias, L0_ffn_c_proj, L0_ffn_proj_bias)
    x = x + jnp.tanh(g_xattn[1]) * _L1_xattn_ref(_layernorm(x, axis=-1), ctx_1024, ctx_1024, mask_BxS2_bf1, L1_xattn_Wq, L1_xattn_bq, L1_xattn_Wk, L1_xattn_bk, L1_xattn_Wv, L1_xattn_bv, L1_xattn_Wo, L1_xattn_bo)
    x = x + jnp.tanh(g_ffn[1]) * _L1_ffn_ref(_layernorm(x, axis=-1), L1_ffn_gate_w, L1_ffn_Wg, L1_ffn_Wu, L1_ffn_Wd, L1_ffn_Ws_g, L1_ffn_Ws_u, L1_ffn_Ws_d)
    return x

_drawn_inputs = setup_inputs


def setup_inputs(seed=0):
    import zlib

    import numpy as np

    out = dict(_drawn_inputs(seed))
    spreads = {'g_ffn': (-1.0, 0.6),
     'L0_ffn_fc_bias': (0.0, 0.681),
     'L0_ffn_proj_bias': (0.0, 0.1),
     'L1_xattn_bq': (0.0, 0.404),
     'L1_xattn_bk': (0.0, 0.8),
     'L1_xattn_bv': (0.0, 0.1),
     'L1_xattn_bo': (0.0, 0.1)}
    factors = {'L0_xattn_Wq': 8.0,
     'L0_xattn_Wk': 8.0,
     'L1_ffn_gate_w': 8.0,
     'L1_ffn_Wg': 8.0,
     'L1_ffn_Wu': 8.0,
     'L1_ffn_Wd': 8.0,
     'L1_ffn_Ws_g': 8.0,
     'L1_ffn_Ws_u': 8.0,
     'L1_ffn_Ws_d': 8.0}
    for name, (base, spread) in spreads.items():
        noise = np.random.default_rng([zlib.crc32(name.encode()), seed]).standard_normal(out[name].shape)
        drawn = base * np.exp(spread * noise) if base else spread * noise
        out[name] = jnp.asarray(drawn.astype(out[name].dtype))
    for name, factor in factors.items():
        out[name] = (out[name] * factor).astype(out[name].dtype)
    return out
```

```python
from contextlib import ExitStack

import numpy as np

import concourse.bass as bass
from concourse import mybir

ALU = mybir.AluOpType
ACT = mybir.ActivationFunctionType
AX = mybir.AxisListType.X
F32 = mybir.dt.float32
BF16 = mybir.dt.bfloat16
U32 = mybir.dt.uint32
U8 = mybir.dt.uint8

P = 128
NB = 16
TK = 77
NH = 16
GH = 4
NG = NH // GH
D0 = 64
D1 = P // NH
BANK = 512
E0 = 8
F0 = 512
CAP0 = int(1.25 * NB * P * 2 / E0)
ST0 = CAP0 // P
E1 = 16
F1 = 256
CAP1 = int(P * 2.0 / E1)
SLOTS1 = E1 * CAP1
TILES0 = E0 * ST0
KEY = 2 * NB * P
ROUND = 1.5 * 2.0 ** 30
MINUS = -10000.0
EPS = 1e-5
KM_CHUNKS = [(0, 6), (6, 5), (11, 5)]
STOP = 4

C_ID, C_TRI, C_HM, C_REV, C_IOTA, C_KEY, C_BLK, C_PI, C_MR, C_END = np.cumsum([0, P, P, NH, E0, P, E0 * ST0, 2 * NB, 1, 1])


def constants():
    c = np.zeros((P, C_END), np.float32)
    c[:, C_ID:C_TRI] = np.eye(P)
    c[:, C_TRI:C_HM] = np.triu(np.ones((P, P)), 1)
    c[np.arange(P), C_HM + np.arange(P) // D1] = 1.0
    c[:, C_REV:C_IOTA] = E0 - np.arange(E0)
    c[:, C_IOTA:C_KEY] = np.arange(P)
    c[:, C_KEY:C_BLK] = (P * np.arange(ST0)[None, :] - KEY * (E0 - np.arange(E0))[:, None]).ravel()
    c[:, C_BLK:C_PI] = 1 + np.arange(2 * NB)
    c[:, C_PI] = np.arange(P)
    c[0, C_MR], c[1, C_MR] = 9984.0, 16.0
    return c


def ge(eng, sem, value):
    if isinstance(value, int) and value <= 0:
        return
    eng.wait_ge(sem, value)


def sweep(eng, n, step):
    step(0, 0)
    step(1, 1)
    with eng.Fori(0, (n - 4) // 2) as i:
        step(i * 2 + 2, 0)
        step(i * 2 + 3, 1)
    step(n - 2, 0)
    step(n - 1, 1)


def is_last(b, n):
    return isinstance(b, int) and b == n - 1


def program(nc, x, ctxT, maskb, gates, consts, w0kq, w0v, w0o, gw0, fc0, fb0, pj0, pb0,
            w1q, w1k, w1v, w1o, b1q, b1k, b1v, b1o, gw1, wg1, wu1, wd1, wsg, wsu, wsd, out):
    xn_dram = nc.dram_tensor("normalised_rows", (NB * P, P), F32, kind="Internal").ap()
    y_dram = nc.dram_tensor("expert_results", (2 * NB * P, P), F32, kind="Internal").ap()

    with ExitStack() as stack:
        def sb(name, shape, dt=F32):
            return stack.enter_context(nc.sbuf_tensor(name, shape, dt))

        def sem(name):
            return stack.enter_context(nc.semaphore(name))

        bank = [stack.enter_context(nc.psum_tensor(f"bank{i}", [P, BANK], F32)) for i in range(8)]

        def part(big, start, shape):
            n = int(np.prod(shape))
            v = big[:, start:start + n]
            if len(shape) > 1:
                names = "abcd"[:len(shape)]
                v = v.rearrange(f"p ({' '.join(names)}) -> p {' '.join(names)}",
                                **{k: s for k, s in zip(names[1:], shape[1:])})
            return v, start + n

        xr = sb("xr", [P, NB, P])
        con = sb("con", [P, int(C_END)])
        ident = con[:, C_ID:C_TRI]
        tri = sb("tri", [P, P], BF16)
        ones = sb("ones", [P, P], BF16)
        gate_t = sb("gate_t", [P, 4])
        gate_raw = sb("gate_raw", [P, 4])
        ctx_sb = sb("ctx_sb", [P, NB * TK])
        st = sb("st", [P, NB, 6])
        mean = sb("mean", [P, NB])
        rstd = sb("rstd", [P, NB])
        lnw = sb("lnw", [P, 6, NB])
        wkq = sb("wkq", [P, 2, 2, P])
        m_sb = sb("m_sb", [P, 2, P])
        big_a = sb("big_a", [P, NB * NH * TK])
        km = big_a[:, :].rearrange("p (b h t) -> p b h t", b=NB, h=NH)
        big_b = sb("big_b", [P, NB * NH * (D0 + 1)])
        v0 = big_b[:, :].rearrange("p (b h d) -> p b h d", b=NB, h=NH)
        wv0 = sb("wv0", [P, NH * D0])
        wo0 = sb("wo0", [P, NH * D0 // P, P])
        xs = sb("xs", [P, 2, P])
        xnT = sb("xnT", [P, 2, P])
        qT = sb("qT", [P, 2, P])
        nmx = sb("nmx", [P, 2, GH])
        pr = sb("pr", [P, 2, GH, TK])
        pT = sb("pT", [P, 2, GH, P])
        rs = sb("rs", [P, 2, GH])
        on = sb("on", [P, 2, NH * D0])
        oT = sb("oT", [P, 2, BANK])
        ytmp = sb("ytmp", [P, P])
        o = 2 * NB * P
        kT1, o = part(big_a, o, (NB, TK))
        kbd, o = part(big_a, o, (2, NH, TK))
        v1, o = part(big_a, o, (NB, NH, D1 + 1))
        mbf, o = part(big_a, o, (NB * TK,))
        after_attention1 = o
        mb8 = sb("mb8", [P, NB * TK], U8)
        mrow = sb("mrow", [P, NB, TK], BF16)
        w1 = sb("w1", [P, 4, P])
        b1 = sb("b1", [P, 2])
        bq1 = sb("bq1", [P, 1])
        b1r = sb("b1r", [P, 2, P])
        gbo = sb("gbo", [P, P])

        o = 0
        xn, o = part(big_b, o, (NB, P))
        xnTa, o = part(big_b, o, (NB, P))
        xe, o = part(big_b, o, (2, ST0, P))
        xeT, o = part(big_b, o, (2, CAP0))
        fc, o = part(big_b, o, (2, F0))
        pj, o = part(big_b, o, (2, F0 // P, P))
        hT, o = part(big_b, o, (2, F0 // P, CAP0))
        ye, o = part(big_b, o, (2, ST0, P))
        assert o <= NB * NH * (D0 + 1)
        yt = big_a[:, 0:2 * NB * P].rearrange("p (k b d) -> p k b d", k=2, b=NB)
        gw0s = sb("gw0s", [P, E0])
        fbr = sb("fbr", [P, 2, F0 // P])
        lg = sb("lg", [P, NB, E0])
        lg2 = sb("lg2", [P, NB, E0])
        rt = sb("rt", [P, NB, E0])
        hot = sb("hot", [P, 2, NB, E0])
        hotb = sb("hotb", [P, 2 * NB, E0], BF16)
        o = after_attention1
        cum, o = part(big_a, o, (2, 2 * NB, E0))
        rk, o = part(big_a, o, (2 * NB, E0))
        pb0s, o = part(big_a, o, (E0, P))
        cumb = sb("cumb", [P, 2 * NB, E0], BF16)
        top = sb("top", [P, 2, NB])
        mp = sb("mp", [P, 2, NB])
        ew = sb("ew", [P, 3, NB])
        rank0 = sb("rank0", [P, 2 * NB])
        tile0 = sb("tile0", [P, 2 * NB])
        pos0 = sb("pos0", [P, 2 * NB])
        key0 = sb("key0", [P, 2 * NB])
        wt0 = sb("wt0", [P, 2, NB])
        row_id = sb("row_id", [P, 3, TILES0])
        idx_put = sb("idx_put", [P, TILES0], U32)
        idx_get = sb("idx_get", [P, TILES0], U32)
        at_pos = big_a[:, 0:NB * P].bitcast(BF16).rearrange("p (n c) -> p n c", c=P)
        in_tile = big_a[:, NB * P:NB * P + 3 * NB * TILES0].bitcast(BF16).rearrange("p (k n c) -> p k n c", k=3, c=TILES0)
        assert 3 * NB * TILES0 <= NB * P
        o = after_attention1
        xn4, o = part(big_a, o, (NB, P))
        xn4T, o = part(big_a, o, (NB, P))
        hot1, o = part(big_a, o, (NB, E1, CAP1))
        o1 = 0
        sc1, o1 = part(big_a, o1, (NB, E1))
        sel1, o1 = part(big_a, o1, (NB, E1))
        pos1, o1 = part(big_a, o1, (NB, E1))
        w1t, o1 = part(big_a, o1, (NB, E1))
        o2 = 0
        xt1, o2 = part(big_b, o2, (E1, NB, CAP1))
        eo1, o2 = part(big_b, o2, (NB, E1, CAP1))
        ohs, o2 = part(big_b, o2, (2, SLOTS1))
        sT, o2 = part(big_b, o2, (2, P))
        sT2, o2 = part(big_b, o2, (2, P))
        g1, o2 = part(big_b, o2, (2, BANK))
        h1, o2 = part(big_b, o2, (2, BANK))
        wgu, o2 = part(big_b, o2, (2, 2, F1))
        wdd, o2 = part(big_b, o2, (2, F1 // P, P))
        ows, o2 = part(big_b, o2, (2, SLOTS1))
        owT, o2 = part(big_b, o2, (2, 2, P))
        eos, o2 = part(big_b, o2, (2, SLOTS1))
        eoT, o2 = part(big_b, o2, (2, 2, P))
        gs, o2 = part(big_b, o2, (2, F1))
        hs, o2 = part(big_b, o2, (2, F1))
        yo, o2 = part(big_b, o2, (2, P))
        assert o <= NB * NH * TK and o2 <= NB * NH * (D0 + 1)
        gw1s = sb("gw1s", [P, E1])
        mx1 = sb("mx1", [P, NB])
        sel1b = sb("sel1b", [P, NB, E1], BF16)
        top8 = sb("top8", [P, 2, 8])
        wss = sb("wss", [P, 3, F1])

        names = """x_in con_in gate_in ctx_in w0v_in w0o_in small_in pb_in mask_in w1_in
            consts_ready gate_ready zero_ready v0_ready pads_ready zero_dram
            wkq_even wkq_odd m_ps m_ready km_ps  km_dve v_ps v_act v_dve
            dve_chain act_chain pool_chain ln_var ln_std stats
            k1_ps k1_act k1_ready v1_ps v1_ready mask_ready
            xn_ready xt_ps xt_ready lg_ps rank_in rank_ps ew_in ew_ready pos_ready key_ready dve_pos lo_ready hi_ready id_ps
            get_ready put_ready rows_out put_even put_odd y_in0 y_in1 y_in2 y_in3
            fe_even fe_odd xe_even xe_odd t_ps t_ready up_ps up_ready dn_ps y_ready x2_ready
            xn4_ready x4_ps x4_ready lg1_ps sc1_in sc1_exp sc1_ready st_ps st_sb sel_ready se_ps
            sel_rows pos_ps hot_ready xst_ready gt_ps gt_ready
            we_even we_odd gu_ps ge_ready h_ready eo_ps eo_ready
            ow_ready es_ready tt_ps tt_ready et_ready sgu_ps sg_ready sh_ready fin_ps y_out_ready out_even out_odd""".split()
        S = {n: sem(n) for n in names}

        def attention_sems(k):
            return {n: sem(f"a{k}_{n}") for n in
                    """xs_ready xt_ps xnT_ready q_ps qT_ready kb_ready sc_ready max_ready sub_ready exp_ready
                    pt_ps pT_ready po_ps rcp_ready on_ready ot_ps oT_ready wo_done x_ready""".split()}

        layers = [
            dict(k=0, dh=D0, nhalf=2, chunks=4, scale=D0 ** -0.5, sem=attention_sems(0), v=v0, wo=wo0, gate=0),
            dict(k=1, dh=D1, nhalf=1, chunks=1, scale=1.0, sem=attention_sems(1), v=v1, wo=w1[:, 3:4, :], gate=1),
        ]
        b_sc, b_pt, b_po, b_ot, b_y, b_xt = bank[0:2], bank[2:4], bank[4], bank[5], bank[6], bank[7]


        def attention_pe(pe, L):
            s, dh, k1 = L["sem"], L["dh"], L["k"] == 1

            def turn_x(b, p):
                pe.wait_ge(s["xs_ready"], b + 1)
                ge(pe, s["qT_ready"] if k1 else s["xnT_ready"], b)
                pe.transpose(b_xt[:, 0:P], xs[:, p, :], ident).then_inc(s["xt_ps"], 1)

            def queries(b, p):
                pe.wait_ge(s["xnT_ready"], b + 1)
                pe.matmul(b_xt[:, 0:P], w1[:, 0, :], xnT[:, p, :], start=True, stop=True).then_inc(s["q_ps"], 1)

            def scores(b, g, p):
                u = b * NG + g
                if g == 0:
                    pe.wait_ge(s["qT_ready"] if k1 else s["xnT_ready"], b + 1)
                    if k1:
                        pe.wait_ge(s["kb_ready"], b + 1)
                ge(pe, s["sub_ready"], u - 1)
                o = b_sc[g % 2][:, 0:GH * TK]
                if k1:
                    pe.matmul(o, qT[:, p, :], kbd[:, p, GH * g:GH * g + GH, :], start=True, stop=False)
                    pe.matmul(o.rearrange("p (h t) -> p h t", h=GH), ones[:, :],
                              mrow[:, b:b + 1, :].broadcast_to([P, GH, TK]) if isinstance(b, int)
                              else mrow[:, bass.ds(b, 1), :].broadcast_to([P, GH, TK]),
                              start=False, stop=True).then_inc(s["sc_ready"], 1)
                else:
                    pe.matmul(o, xnT[:, p, :], km[:, b, GH * g:GH * g + GH, :],
                              start=True, stop=True).then_inc(s["sc_ready"], 1)

            def turn_p(b, g):
                u = b * NG + g
                pe.wait_ge(s["exp_ready"], u + 1)
                ge(pe, s["pT_ready"], u - 1)
                for h in range(GH):
                    last = pe.transpose(b_pt[g % 2][0:TK, P * h:P * h + P], pr[:, g % 2, h, :], ident)
                last.then_inc(s["pt_ps"], 1)

            def values(b, g):
                u = b * NG + g
                pe.wait_ge(s["pT_ready"], u + 1)
                ge(pe, s["on_ready"], u)
                for h in range(GH):
                    last = pe.matmul(b_po[:, h * (dh + 1):(h + 1) * (dh + 1)], pT[:, g % 2, h, :],
                                     L["v"][:, b, GH * g + h, :], start=True, stop=True)
                last.then_inc(s["po_ps"], 1)

            nhalf, chunks = L["nhalf"], L["chunks"]

            def turn_o(b, p, hf):
                n = b * nhalf + hf
                pe.wait_ge(s["on_ready"], b * NG + (hf + 1) * (NG // nhalf))
                ge(pe, s["oT_ready"], n)
                for c in range(chunks):
                    at = P * (hf * chunks + c)
                    last = pe.transpose(b_ot[:, P * c:P * c + P], on[:, p, at:at + P], ident)
                last.then_inc(s["ot_ps"], 1)

            def project(b, hf):
                n = b * nhalf + hf
                pe.wait_ge(s["oT_ready"], n + 1)
                if hf == 0:
                    ge(pe, s["x_ready"], b)
                for c in range(chunks):
                    last = pe.matmul(b_y[:, 0:P], oT[:, hf, P * c:P * c + P], L["wo"][:, hf * chunks + c, :],
                                     start=(hf == 0 and c == 0), stop=(hf == nhalf - 1 and c == chunks - 1))
                last.then_inc(s["wo_done"], 1)

            turn_x(0, 0)
            if k1:
                queries(0, 0)
            scores(0, 0, 0)

            def batch(b, p):
                first, last = isinstance(b, int) and b == 0, is_last(b, NB)
                for g in range(NG):
                    if g < NG - 1:
                        scores(b, g + 1, p)
                    elif not last:
                        scores(b + 1, 0, 1 - p)
                    turn_p(b, g)
                    if g > 0:
                        values(b, g - 1)
                    elif not first:
                        values(b - 1, NG - 1)
                    if not last and g == 0:
                        turn_x(b + 1, 1 - p)
                    if not last and k1 and g == 1:
                        queries(b + 1, 1 - p)
                    if not first:
                        if nhalf == 2 and g == 0:
                            turn_o(b - 1, 1 - p, 0)
                        if nhalf == 2 and g == 1:
                            project(b - 1, 0)
                        if g == 1:
                            turn_o(b - 1, 1 - p, nhalf - 1)
                        if g == 2:
                            project(b - 1, nhalf - 1)

            sweep(pe, NB, batch)
            values(NB - 1, NG - 1)
            for hf in range(nhalf):
                turn_o(NB - 1, 1, hf)
                project(NB - 1, hf)

        def attention_dve(dve, L):
            s, dh, k1, nhalf = L["sem"], L["dh"], L["k"] == 1, L["nhalf"]

            def stage(b, p):
                ge(dve, s["xt_ps"], b - 1)
                nc.vector.tensor_scalar(xs[:, p, :], xr[:, b, :], mean[:, b:b + 1] if isinstance(b, int) else mean[:, bass.ds(b, 1)],
                                        rstd[:, b:b + 1] if isinstance(b, int) else rstd[:, bass.ds(b, 1)],
                                        ALU.subtract, ALU.mult).then_inc(s["xs_ready"], 1)

            def softmax_in(b, g):
                u = b * NG + g
                dve.wait_ge(s["sc_ready"], u + 1)
                ge(dve, s["sub_ready"], u - 1)
                sc = b_sc[g % 2][:, 0:GH * TK].rearrange("p (h t) -> p h t", h=GH)
                nc.vector.tensor_reduce(nmx[:, g % 2, :], sc, AX, ALU.max, negate=True).then_inc(s["max_ready"], 1)
                dve.wait_ge(s["max_ready"], u + 1)
                ge(dve, s["pt_ps"], u - 1)
                nc.vector.tensor_tensor(pr[:, g % 2, :, :], sc,
                                        nmx[:, g % 2, :].unsqueeze(2).broadcast_to([P, GH, TK]),
                                        ALU.add).then_inc(s["sub_ready"], 1)

            def normalise(b, g, p):
                u = b * NG + g
                dve.wait_ge(s["po_ps"], u + 1)
                ge(dve, s["on_ready"], u - 1)
                po = b_po[:, 0:GH * (dh + 1)].rearrange("p (h d) -> p h d", h=GH)
                nc.vector.reciprocal(rs[:, g % 2, :], po[:, :, dh]).then_inc(s["rcp_ready"], 1)
                dve.wait_ge(s["rcp_ready"], u + 1)
                if g == 0:
                    ge(dve, s["ot_ps"], (b - 1) * nhalf)
                o = on[:, p, GH * g * dh:GH * (g + 1) * dh].rearrange("p (h d) -> p h d", h=GH)
                nc.vector.tensor_tensor(o, po[:, :, 0:dh], rs[:, g % 2, :].unsqueeze(2).broadcast_to([P, GH, dh]),
                                        ALU.mult).then_inc(s["on_ready"], 1)

            def residual(b):
                dve.wait_ge(s["wo_done"], (b + 1) * nhalf)
                gt = gate_t[:, L["gate"]:L["gate"] + 1]
                if k1:
                    ge(dve, s["x_ready"], b)
                    nc.vector.scalar_tensor_tensor(ytmp[:, :], b_y[:, 0:P], gt, gbo[:, :], ALU.mult,
                                                   ALU.add).then_inc(S["dve_chain"], 1)
                    chain[0] += 1
                    dve.wait_ge(S["dve_chain"], chain_at(b))
                    nc.vector.tensor_tensor(xr[:, b, :], ytmp[:, :], xr[:, b, :], ALU.add).then_inc(s["x_ready"], 1)
                else:
                    nc.vector.scalar_tensor_tensor(xr[:, b, :], b_y[:, 0:P], gt, xr[:, b, :], ALU.mult,
                                                   ALU.add).then_inc(s["x_ready"], 1)

            def stats_of(b):
                dve.wait_ge(s["x_ready"], b + 1)
                nc.vector.bn_stats(st[:, b, :], xr[:, b, :]).then_inc(S["stats"], 1)

            base = chain[0]

            def chain_at(b):
                return b + (base + 1)

            stage(0, 0)

            def batch(b, p):
                first, last = isinstance(b, int) and b == 0, is_last(b, NB)
                for g in range(NG):
                    softmax_in(b, g)
                    if g == 0 and not last:
                        stage(b + 1, 1 - p)
                    if g > 1:
                        normalise(b, g - 2, p)
                    elif not first:
                        normalise(b - 1, g + 2, 1 - p)
                    if g == 3 and not first:
                        residual(b - 1)
                        stats_of(b - 1)

            sweep(dve, NB, batch)
            normalise(NB - 1, 2, 1)
            normalise(NB - 1, 3, 1)
            residual(NB - 1)
            stats_of(NB - 1)
            chain[0] = base + (NB if k1 else 0)

        def attention_act(act, L):
            s, k1, nhalf, chunks = L["sem"], L["k"] == 1, L["nhalf"], L["chunks"]

            def x_out(b, p):
                act.wait_ge(s["xt_ps"], b + 1)
                if k1:
                    ge(act, s["q_ps"], b - 1)
                else:
                    ge(act, s["sc_ready"], (b - 1) * NG)
                nc.scalar.activation(xnT[:, p, :], b_xt[:, 0:P], ACT.Copy).then_inc(s["xnT_ready"], 1)

            def q_out(b, p):
                act.wait_ge(s["q_ps"], b + 1)
                ge(act, s["sc_ready"], (b - 1) * NG)
                nc.scalar.activation(qT[:, p, :], b_xt[:, 0:P], ACT.Identity, bias=bq1[:, :],
                                     scale=D1 ** -0.5).then_inc(s["qT_ready"], 1)

            def o_out(b, hf):
                n = b * nhalf + hf
                act.wait_ge(s["ot_ps"], n + 1)
                if nhalf == 2:
                    ge(act, s["wo_done"], n - 1)
                else:
                    ge(act, s["wo_done"], n)
                nc.scalar.activation(oT[:, hf, 0:P * chunks], b_ot[:, 0:P * chunks],
                                     ACT.Copy).then_inc(s["oT_ready"], 1)

            x_out(0, 0)
            if k1:
                q_out(0, 0)

            def batch(b, p):
                first, last = isinstance(b, int) and b == 0, is_last(b, NB)
                for g in range(NG):
                    u = b * NG + g
                    act.wait_ge(s["sub_ready"], u + 1)
                    nc.scalar.activation(pr[:, g % 2, :, :], pr[:, g % 2, :, :], ACT.Exp,
                                         scale=L["scale"]).then_inc(s["exp_ready"], 1)
                    act.wait_ge(s["pt_ps"], u + 1)
                    ge(act, s["po_ps"], u - 1)
                    nc.scalar.activation(pT[0:TK, g % 2, :, :],
                                         b_pt[g % 2][0:TK, :].rearrange("p (h q) -> p h q", h=GH),
                                         ACT.Copy).then_inc(s["pT_ready"], 1)
                    if not last and g == 0:
                        x_out(b + 1, 1 - p)
                    if not last and k1 and g == 1:
                        q_out(b + 1, 1 - p)
                    if not first:
                        if nhalf == 2 and g == 0:
                            o_out(b - 1, 0)
                        if g == 1:
                            o_out(b - 1, nhalf - 1)

            sweep(act, NB, batch)
            for hf in range(nhalf):
                o_out(NB - 1, hf)

        chain = [0]

        def link(dve, ins):
            chain[0] += 1
            ins.then_inc(S["dve_chain"], 1)
            dve.wait_ge(S["dve_chain"], chain[0])

        ln_turn = [0]

        def layer_norm(dve):
            ln_turn[0] += 1
            me, mo, cve, cvo = (st[:, :, i] for i in (1, 4, 2, 5))
            sm, df, cv, var = (lnw[:, i, :] for i in range(4))
            v = nc.vector
            dve.wait_ge(S["stats"], NB * ln_turn[0])
            link(dve, v.tensor_tensor(sm, me, mo, ALU.add))
            link(dve, v.tensor_tensor(df, me, mo, ALU.subtract))
            link(dve, v.tensor_tensor(cv, cve, cvo, ALU.add))
            link(dve, v.tensor_scalar(mean[:, :], sm, 0.5, None, ALU.mult))
            link(dve, v.tensor_tensor(df, df, df, ALU.mult))
            link(dve, v.scalar_tensor_tensor(cv, df, P / 4.0, cv, ALU.mult, ALU.add))
            v.tensor_scalar(var, cv, 1.0 / P, EPS, ALU.mult, ALU.add).then_inc(S["ln_var"], 1)
            dve.wait_ge(S["ln_std"], ln_turn[0])
            rough, sq = lnw[:, 5, :], lnw[:, 0, :]
            link(dve, v.reciprocal(rough, lnw[:, 4, :]))
            link(dve, v.tensor_tensor(sq, rough, rough, ALU.mult))
            link(dve, v.tensor_tensor(sq, sq, var, ALU.mult))
            link(dve, v.tensor_scalar(sq, sq, -0.5, 1.5, ALU.mult, ALU.add))
            link(dve, v.tensor_tensor(rstd[:, :], sq, rough, ALU.mult))

        def layer_norm_root(act, n):
            act.wait_ge(S["ln_var"], n)
            nc.scalar.activation(lnw[:, 4, :], lnw[:, 3, :], ACT.Sqrt).then_inc(S["ln_std"], 1)

        block = stack.enter_context(nc.Block())

        @block.sync
        def _(sp):
            sp.dma_start(xr[:, :, :], x.rearrange("(b p) d -> p b d", p=P)).then_inc(S["x_in"], 16)
            sp.dma_start(con[:, :], consts).then_inc(S["con_in"], 16)
            sp.dma_start(ctx_sb[:, :], ctxT).then_inc(S["ctx_in"], 16)
            sp.dma_start(gate_raw[:, :], gates.rearrange("(o g) -> o g", o=1).broadcast_to([P, 4])).then_inc(S["gate_in"], 16)

            sp.wait_ge(S["pads_ready"], 1)

            def head(h, p):
                ge(sp, S["m_ps"], h - 1)
                src = w0kq[h] if isinstance(h, int) else w0kq[h]
                sp.dma_start(wkq[0:D0, p, :, :], src).then_inc(S["wkq_odd" if p else "wkq_even"], 16)
            sweep(sp, NH, head)
            sp.dma_start(wv0[:, :], w0v).then_inc(S["w0v_in"], 16)
            sp.dma_start(wo0[:, :, :], w0o.rearrange("(c p) d -> p c d", p=P)).then_inc(S["w0o_in"], 16)
            for i, w in enumerate((w1q, w1k, w1v, w1o)):
                sp.dma_start(w1[:, i, :], w).then_inc(S["w1_in"], 16)
            for i, w in enumerate((b1q, b1k)):
                sp.dma_start(b1[:, i:i + 1], w.rearrange("(p o) -> p o", o=1)).then_inc(S["w1_in"], 16)
            for i, w in enumerate((b1v, b1o)):
                sp.dma_start(b1r[:, i, :], w.rearrange("(o d) -> o d", o=1).broadcast_to([P, P])).then_inc(S["w1_in"], 16)
            sp.dma_start(mb8[:, :], maskb.rearrange("(o t) -> o t", o=1).broadcast_to([P, NB * TK])).then_inc(S["mask_in"], 16)
            sp.dma_start(gw0s[:, :], gw0).then_inc(S["small_in"], 16)
            sp.dma_start(gw1s[:, :], gw1).then_inc(S["small_in"], 16)
            sp.dma_start(wss[:, 0, :], wsg).then_inc(S["small_in"], 16)
            sp.dma_start(wss[:, 1, :], wsu).then_inc(S["small_in"], 16)
            sp.dma_start(wss[:, 2, :].rearrange("p (c d) -> p c d", c=F1 // P),
                         wsd.rearrange("(c p) d -> p c d", p=P)).then_inc(S["small_in"], 16)

            if STOP >= 2:
                for q in range(NB // 4):
                    sp.wait_ge(S["xn_ready"], 4 * q + 4)
                    sp.dma_start(xn_dram.rearrange("(b p) d -> p b d", p=P)[:, 4 * q:4 * q + 4, :],
                                 xn[:, 4 * q:4 * q + 4, :]).then_inc(S["rows_out"], 16)
                sp.dma_start(pb0s[:, :, :], pb0.rearrange("(o e) d -> o e d", o=1).broadcast_to([P, E0, P])).then_inc(S["pb_in"], 16)

                def expert(e, p):
                    ge(sp, S["dn_ps"], (e - 1) * 2)
                    sp.dma_start(fbr[:, p, :], fb0[e]).then_inc(S["fe_odd" if p else "fe_even"], 16)
                    sp.dma_start(fc[:, p, :], fc0[e]).then_inc(S["fe_odd" if p else "fe_even"], 16)
                    sp.dma_start(pj[:, p, :, :], pj0[e].rearrange("(c p) d -> p c d", p=P)).then_inc(S["fe_odd" if p else "fe_even"], 16)
                sweep(sp, E0, expert)

                sp.wait_ge(S["put_even"], 16 * ST0 * E0 // 2)
                sp.wait_ge(S["put_odd"], 16 * ST0 * E0 // 2)
                for q in range(4):
                    for k in range(2):
                        sp.dma_start(yt[:, k, 4 * q:4 * q + 4, :],
                                     y_dram.rearrange("(k b p) d -> k p b d", k=2, p=P)[k][:, 4 * q:4 * q + 4, :]
                                     ).then_inc(S[f"y_in{q}"], 16)

            if STOP >= 4:
                sp.wait_ge(S["x2_ready"], 2 * NB)

                def expert1(e, p):
                    ge(sp, S["eo_ps"], e - 1)
                    w = S["we_odd" if p else "we_even"]
                    sp.dma_start(wgu[:, p, 0, :], wg1[e]).then_inc(w, 16)
                    sp.dma_start(wgu[:, p, 1, :], wu1[e]).then_inc(w, 16)
                    sp.dma_start(wdd[:, p, :, :], wd1[e].rearrange("(c p) d -> p c d", p=P)).then_inc(w, 16)
                sweep(sp, E1, expert1)

                def put_out(b, p):
                    sp.wait_ge(S["y_out_ready"], b + 1)
                    sp.dma_start(out.rearrange("(b p) d -> b p d", p=P)[b], yo[:, p, :]).then_inc(S["out_odd" if p else "out_even"], 16)
                sweep(sp, NB, put_out)
                sp.wait_ge(S["out_even"], 16 * NB // 2)
                sp.wait_ge(S["out_odd"], 16 * NB // 2)
            else:
                if STOP == 1:
                    sp.wait_ge(S["stats"], NB * 2)
                if STOP == 2:
                    sp.wait_ge(S["stats"], NB * 3)
                if STOP == 3:
                    sp.wait_ge(S["stats"], NB * 4)
                sp.dma_start(out.rearrange("(b p) d -> p b d", p=P), xr[:, :, :]).then_inc(S["out_even"], 16)
                sp.wait_ge(S["out_even"], 16)

        @block.gpsimd
        def _(pool):
            g = nc.gpsimd
            g.memset(wkq[:, :, :, :], 0.0).then_inc(S["pads_ready"], 1)
            g.memset(big_b[:, :], 0.0).then_inc(S["v0_ready"], 1)
            g.memset(pT[:, :, :, :], 0.0).then_inc(S["zero_ready"], 1)
            pool.wait_ge(S["v0_ready"], 1)
            pool.dma_start(y_dram.rearrange("(p k) d -> p (k d)", p=P), big_b[:, 0:2 * NB * P]).then_inc(S["zero_dram"], 16)
            g.memset(ones[:, :], 1.0).then_inc(S["zero_ready"], 1)
            pool.wait_ge(S["zero_dram"], 16)
            g.memset(v0[:, :, :, D0:D0 + 1], 1.0).then_inc(S["v0_ready"], 1)

            if STOP >= 2:
                pool.wait_ge(layers[0]["sem"]["sc_ready"], NB * NG)
                g.memset(v1[:, :, :, :], 0.0).then_inc(S["pool_chain"], 1)
                pool.wait_ge(S["pool_chain"], 1)
                g.memset(v1[:, :, :, D1:D1 + 1], 1.0).then_inc(S["pool_chain"], 1)
                pool.wait_ge(S["key_ready"], 1)
                g.tensor_tensor(in_tile[:, 1, :, :], in_tile[:, 0, :, :],
                                con[:, C_BLK:C_PI].unsqueeze(2).broadcast_to([P, 2 * NB, TILES0]),
                                ALU.mult).then_inc(S["hi_ready"], 1)

                def rows_in(e):
                    if e >= 2:
                        pool.wait_ge(S["t_ps"], e - 1)
                    for t in range(ST0):
                        n = e * ST0 + t
                        pool.indirect_dma_start(xe[:, e % 2, t, :], None, xn_dram,
                                                bass.IndirectOffsetOnAxis(ap=idx_get[:, n:n + 1], axis=0),
                                                bounds_check=NB * P - 1, oob_is_err=False
                                                ).then_inc(S["xe_odd" if e % 2 else "xe_even"], 16)

                def results_out(e):
                    pool.wait_ge(S["y_ready"], e * 2 + 2)
                    for t in range(ST0):
                        n = e * ST0 + t
                        pool.indirect_dma_start(y_dram, bass.IndirectOffsetOnAxis(ap=idx_put[:, n:n + 1], axis=0),
                                                ye[:, e % 2, t, :], None, bounds_check=2 * NB * P - 1,
                                                oob_is_err=False).then_inc(S["put_odd" if e % 2 else "put_even"], 16)

                pool.wait_ge(S["rows_out"], 16 * NB // 4)
                pool.wait_ge(S["get_ready"], 1)
                for e in range(3):
                    rows_in(e)
                pool.wait_ge(S["put_ready"], 1)
                for e in range(E0):
                    results_out(e)
                    if e + 3 < E0:
                        rows_in(e + 3)
            if STOP >= 3:
                s = layers[1]["sem"]
                pool.wait_ge(S["k1_ready"], 1)

                def keys(b, p):
                    ge(pool, s["sc_ready"], (b - 1) * NG)
                    kb = kT1[:, b:b + 1, :] if isinstance(b, int) else kT1[:, bass.ds(b, 1), :]
                    g.tensor_tensor(kbd[:, p, :, :], kb.broadcast_to([P, NH, TK]),
                                    con[:, C_HM:C_REV].unsqueeze(2).broadcast_to([P, NH, TK]),
                                    ALU.mult).then_inc(s["kb_ready"], 1)
                sweep(pool, NB, keys)
            if STOP >= 4:
                pool.wait_ge(S["xn4_ready"], NB)

                def rows(b, p):
                    ge(pool, S["gt_ps"], b - 1)
                    g.tensor_copy(xs[:, p, :], xn4[:, b, :]).then_inc(S["xst_ready"], 1)
                sweep(pool, NB, rows)
                pool.wait_ge(S["eo_ready"], E1)

                def results(b, p):
                    ge(pool, S["tt_ps"], b - 1)
                    g.tensor_copy(eos[:, p, :], eo1[:, b, :, :].rearrange("p e c -> p (e c)")).then_inc(S["es_ready"], 1)
                sweep(pool, NB, results)

        @block.scalar
        def _(act):
            a = nc.scalar
            layer_norm_root(act, 1)
            act.wait_ge(S["gate_in"], 16)
            a.activation(gate_t[:, :], gate_raw[:, :], ACT.Tanh).then_inc(S["gate_ready"], 1)

            def m_out(h, p):
                act.wait_ge(S["m_ps"], h + 1)
                ge(act, S["km_ps"], (h - 1) * 3)
                a.activation(m_sb[:, p, :], bank[p][:, 0:P], ACT.Copy).then_inc(S["m_ready"], 1)

            m_out(0, 0)

            def head(h, p):
                if not is_last(h, NH):
                    m_out(h + 1, 1 - p)
            sweep(act, NH, head)
            act.wait_ge(S["v0_ready"], 2)
            for b in range(NB):
                act.wait_ge(S["v_ps"], 2 * b + 2)
                a.activation(v0[0:TK, b, 8:16, 0:D0], bank[(2 * b + 1) % 8][0:TK, :].rearrange("p (h d) -> p h d", h=8),
                             ACT.Copy).then_inc(S["v_act"], 1)
            act.wait_ge(S["zero_ready"], 2)
            attention_act(act, layers[0])

            if STOP >= 2:
                layer_norm_root(act, 2)
                for q in range(NB // 4):
                    act.wait_ge(S["xt_ps"], q + 1)
                    a.activation(xnTa[:, 4 * q:4 * q + 4, :], bank[q % 2][:, :].rearrange("p (b t) -> p b t", b=4),
                                 ACT.Copy).then_inc(S["xt_ready"], 1)
                act.wait_ge(S["ew_in"], 1)
                a.activation(ew[:, 1, :], ew[:, 0, :], ACT.Exp).then_inc(S["ew_ready"], 1)
                act.wait_ge(S["w1_in"], 16 * 8)
                for c, (b0, nb) in enumerate(KM_CHUNKS):
                    act.wait_ge(S["k1_ps"], c + 1)
                    a.activation(kT1[:, b0:b0 + nb, :], bank[4 + c][:, 0:nb * TK].rearrange("p (b t) -> p b t", b=nb),
                                 ACT.Identity, bias=b1[:, 1:2]).then_inc(S["k1_act"], 1)
                act.wait_ge(S["key_ready"], 1)
                a.activation(in_tile[:, 2, :, :], in_tile[:, 0, :, :], ACT.Copy,
                             scale=con[:, C_PI:C_PI + 1]).then_inc(S["lo_ready"], 1)

                def expert(e, p):
                    act.wait_ge(S["fe_odd" if p else "fe_even"], (e - p) * 24 + 48)
                    for n in range(8):
                        act.wait_ge(S["up_ps"], e * 8 + n + 1)
                        if n == 0:
                            ge(act, S["dn_ps"], (e - 1) * 2)
                        c, w = n // 2, n % 2
                        a.activation(hT[:, p, c, 320 * w:320 * w + 320], bank[2 + n % 4][:, 0:320], ACT.Gelu,
                                     bias=fbr[:, p, c:c + 1]).then_inc(S["up_ready"], 1)
                act.wait_ge(S["small_in"], 16 * 5)
                sweep(act, E0, expert)
            if STOP >= 3:
                layer_norm_root(act, 3)
                attention_act(act, layers[1])
            if STOP >= 4:
                layer_norm_root(act, 4)
                for q in range(NB // 4):
                    act.wait_ge(S["x4_ps"], q + 1)
                    a.activation(xn4T[:, 4 * q:4 * q + 4, :], bank[q % 2][:, :].rearrange("p (b t) -> p b t", b=4),
                                 ACT.Copy).then_inc(S["x4_ready"], 1)
                act.wait_ge(S["sc1_in"], 1)
                a.activation(sc1[:, :, :], sc1[:, :, :], ACT.Exp).then_inc(S["sc1_exp"], 1)
                act.wait_ge(S["st_ps"], 1)
                a.activation(sT[:, :, :], bank[3][:, 0:2 * P].rearrange("p (k t) -> p k t", k=2),
                             ACT.Copy).then_inc(S["st_sb"], 1)

                def expert1(e, p):
                    act.wait_ge(S["gu_ps"], e + 1)
                    ge(act, S["h_ready"], e - 1)
                    a.activation(g1[:, p, :], bank[p][:, :], ACT.Gelu).then_inc(S["ge_ready"], 1)
                sweep(act, E1, expert1)

                def batch1(b, p):
                    act.wait_ge(S["tt_ps"], b + 1)
                    ge(act, S["fin_ps"], b - 1)
                    a.activation(eoT[:, p, :, :], bank[2 + p][:, 0:2 * P].rearrange("p (k d) -> p k d", k=2),
                                 ACT.Copy).then_inc(S["et_ready"], 1)
                    act.wait_ge(S["sgu_ps"], b + 1)
                    ge(act, S["sh_ready"], b - 1)
                    a.activation(gs[:, p, :], bank[4 + p][:, 0:F1], ACT.Gelu).then_inc(S["sg_ready"], 1)
                sweep(act, NB, batch1)

        @block.vector
        def _(dve):
            v = nc.vector
            dve.wait_ge(S["x_in"], 16)
            for b in range(NB):
                v.bn_stats(st[:, b, :], xr[:, b, :]).then_inc(S["stats"], 1)
            layer_norm(dve)
            dve.wait_ge(S["con_in"], 16)
            v.tensor_copy(tri[:, :], con[:, C_TRI:C_HM]).then_inc(S["consts_ready"], 1)

            def head(h, p):
                for c, (b0, nb) in enumerate(KM_CHUNKS):
                    dve.wait_ge(S["km_ps"], h * 3 + c + 1)
                    v.tensor_copy(km[:, b0:b0 + nb, h, :], bank[2 + 3 * p + c][:, 0:nb * TK].rearrange("p (b t) -> p b t", b=nb)
                                  ).then_inc(S["km_dve"], 1)
            sweep(dve, NH, head)
            dve.wait_ge(S["v0_ready"], 2)
            for b in range(NB):
                dve.wait_ge(S["v_ps"], 2 * b + 1)
                v.tensor_copy(v0[0:TK, b, 0:8, 0:D0], bank[2 * b % 8][0:TK, :].rearrange("p (h d) -> p h d", h=8)
                              ).then_inc(S["v_dve"], 1)
            dve.wait_ge(S["gate_ready"], 1)
            attention_dve(dve, layers[0])

            if STOP >= 2:
                layer_norm(dve)
                dve.wait_ge(layers[0]["sem"]["po_ps"], NB * NG)
                for b in range(NB):
                    v.tensor_scalar(xn[:, b, :], xr[:, b, :], mean[:, b:b + 1], rstd[:, b:b + 1],
                                    ALU.subtract, ALU.mult).then_inc(S["xn_ready"], 1)

                def wide(a, n=NB):
                    return a.unsqueeze(2).broadcast_to([P, n, E0])

                def row(a, n=NB):
                    return con[:, a:a + E0].unsqueeze(1).broadcast_to([P, n, E0])

                dve.wait_ge(S["lg_ps"], 1)
                link(dve, v.tensor_copy(lg[:, :, :], bank[2][:, 0:NB * E0].rearrange("p (b e) -> p b e", b=NB)))
                cur = lg
                for k in range(2):
                    link(dve, v.tensor_reduce(top[:, k, :], cur[:, :, :], AX, ALU.max))
                    link(dve, v.tensor_tensor(rt[:, :, :], cur[:, :, :], wide(top[:, k, :]), ALU.is_equal))
                    link(dve, v.tensor_tensor(rt[:, :, :], rt[:, :, :], row(C_REV), ALU.mult))
                    link(dve, v.tensor_reduce(mp[:, k, :], rt[:, :, :], AX, ALU.max))
                    link(dve, v.tensor_tensor(hot[:, k, :, :], rt[:, :, :], wide(mp[:, k, :]), ALU.is_equal))
                    if k == 0:
                        link(dve, v.scalar_tensor_tensor(lg2[:, :, :], hot[:, 0, :, :], -3.0e38, lg[:, :, :],
                                                         ALU.mult, ALU.add))
                        cur = lg2
                v.tensor_tensor(ew[:, 0, :], top[:, 1, :], top[:, 0, :], ALU.subtract).then_inc(S["ew_in"], 1)
                hf = hot[:, :, :, :].rearrange("p k b e -> p (k b) e")
                v.tensor_copy(hotb[:, :, :], hf).then_inc(S["rank_in"], 1)
                link(dve, v.memset(cum[:, 0, 0:1, :], 0.0))
                link(dve, v.tensor_copy(cum[:, 0, 1:, :], hf[:, 0:2 * NB - 1, :]))
                step, a = 1, 0
                while step < 2 * NB:
                    link(dve, v.tensor_copy(cum[:, 1 - a, 0:step, :], cum[:, a, 0:step, :]))
                    link(dve, v.tensor_tensor(cum[:, 1 - a, step:, :], cum[:, a, step:, :],
                                              cum[:, a, 0:2 * NB - step, :], ALU.add))
                    step, a = 2 * step, 1 - a
                v.tensor_copy(cumb[:, :, :], cum[:, a, :, :]).then_inc(S["rank_in"], 1)
                dve.wait_ge(S["rank_ps"], 1)
                rank = bank[3][:, 0:2 * NB * E0].rearrange("p (n e) -> p n e", e=E0)
                link(dve, v.tensor_tensor(rk[:, :, :], rank, hf, ALU.mult))
                link(dve, v.tensor_reduce(rank0[:, :], rk[:, :, :], AX, ALU.add))
                link(dve, v.tensor_scalar(tile0[:, :], rank0[:, :], 0.25 - P / 2, ROUND, ALU.add, ALU.add))
                link(dve, v.tensor_scalar(tile0[:, :], tile0[:, :], -ROUND, None, ALU.add))
                v.tensor_tensor(pos0[:, :], rank0[:, :], tile0[:, :], ALU.subtract).then_inc(S["pos_ready"], 1)
                link(dve, v.scalar_tensor_tensor(key0[:, :], mp[:, :, :].rearrange("p k b -> p (k b)"), -float(KEY),
                                                 tile0[:, :], ALU.mult, ALU.add))
                v.tensor_tensor(in_tile[:, 0, :, :], key0[:, :].unsqueeze(2).broadcast_to([P, 2 * NB, TILES0]),
                                con[:, C_KEY:C_BLK].unsqueeze(1).broadcast_to([P, 2 * NB, TILES0]),
                                ALU.is_equal).then_inc(S["key_ready"], 1)
                dve.wait_ge(S["pos_ready"], 1)
                for r in range(0, 2 * NB, 8):
                    v.tensor_tensor(at_pos[:, r:r + 8, :], pos0[:, r:r + 8].unsqueeze(2).broadcast_to([P, 8, P]),
                                    con[:, C_IOTA:C_KEY].unsqueeze(1).broadcast_to([P, 8, P]),
                                    ALU.is_equal).then_inc(S["dve_pos"], 1)
                dve.wait_ge(S["id_ps"], 1)
                ids = bank[2][:, BANK // 2:BANK // 2 + 2 * TILES0].rearrange("p (k n) -> p k n", k=2)
                link(dve, v.tensor_copy(row_id[:, 1, :], ids[:, 1, :]))
                link(dve, v.scalar_tensor_tensor(row_id[:, 0, :], ids[:, 0, :], float(P), row_id[:, 1, :],
                                                 ALU.mult, ALU.add))
                link(dve, v.tensor_scalar(row_id[:, 1, :], row_id[:, 0, :], float(P + NB * P), -float(NB * P),
                                          ALU.is_ge, ALU.mult))
                link(dve, v.scalar_tensor_tensor(row_id[:, 1, :], row_id[:, 0, :], -float(P), row_id[:, 1, :],
                                                 ALU.add, ALU.add))
                link(dve, v.tensor_scalar(row_id[:, 1, :], row_id[:, 1, :], 0.0, None, ALU.max))
                v.tensor_copy(idx_get[:, :], row_id[:, 1, :]).then_inc(S["get_ready"], 1)
                link(dve, v.tensor_scalar(row_id[:, 2, :], row_id[:, 0, :], float(P), 65536.0, ALU.is_lt, ALU.mult))
                link(dve, v.scalar_tensor_tensor(row_id[:, 2, :], row_id[:, 0, :], -float(P), row_id[:, 2, :],
                                                 ALU.add, ALU.add))
                dve.wait_ge(S["zero_dram"], 16)
                v.tensor_copy(idx_put[:, :], row_id[:, 2, :]).then_inc(S["put_ready"], 1)
                dve.wait_ge(S["ew_ready"], 1)
                link(dve, v.tensor_scalar(ew[:, 2, :], ew[:, 1, :], 1.0, None, ALU.add))
                link(dve, v.reciprocal(ew[:, 0, :], ew[:, 2, :]))
                link(dve, v.tensor_scalar(wt0[:, 0, :], ew[:, 0, :], gate_t[:, 2:3], None, ALU.mult))
                link(dve, v.tensor_tensor(wt0[:, 1, :], wt0[:, 0, :], ew[:, 1, :], ALU.mult))

                dve.wait_ge(S["mask_in"], 16)
                link(dve, v.tensor_copy(mbf[:, :], mb8[:, :]))
                v.tensor_scalar(mrow[:, :, :].rearrange("p b t -> p (b t)"), mbf[:, :], 1.0, con[:, C_MR:C_MR + 1],
                                ALU.subtract, ALU.mult).then_inc(S["mask_ready"], 1)
                dve.wait_ge(S["k1_act"], 3)
                kf = kT1[:, :, :].rearrange("p b t -> p (b t)")
                v.tensor_tensor(kf, kf, mbf[:, :], ALU.mult).then_inc(S["k1_ready"], 1)
                link(dve, v.tensor_scalar(bq1[:, :], b1[:, 0:1], D1 ** -0.5, None, ALU.mult))
                link(dve, v.tensor_scalar(gbo[:, :], b1r[:, 1, :], gate_t[:, 1:2], None, ALU.mult))
                dve.wait_ge(S["pool_chain"], 2)
                for q in range(NB // 4):
                    dve.wait_ge(S["v1_ps"], q + 1)
                    for r in range(4):
                        v.tensor_tensor(v1[0:TK, 4 * q + r, :, 0:D1],
                                        bank[4 + q][0:TK, P * r:P * r + P].rearrange("p (h d) -> p h d", h=NH),
                                        b1r[0:TK, 0, :].rearrange("p (h d) -> p h d", h=NH), ALU.add
                                        ).then_inc(S["v1_ready"], 1)
                dve.wait_ge(S["small_in"], 16 * 5)

                def turned(e, p):
                    dve.wait_ge(S["t_ps"], e + 1)
                    ge(dve, S["up_ps"], (e - 1) * 8)
                    v.tensor_copy(xeT[:, p, 0:BANK], bank[0][:, :]).then_inc(S["t_ready"], 1)
                    v.tensor_copy(xeT[:, p, BANK:CAP0], bank[1][:, 0:P]).then_inc(S["t_ready"], 1)

                turned(0, 0)

                def expert(e, p):
                    if not is_last(e, E0):
                        turned(e + 1, 1 - p)
                    pe_ = pb0s[:, e, :]
                    if isinstance(e, int) and e == 0:
                        dve.wait_ge(S["pb_in"], 16)
                    dve.wait_ge(S["dn_ps"], e * 2 + 1)
                    ge(dve, S["put_odd" if p else "put_even"], (e - p) * (8 * ST0))
                    pbw = pb0s[:, e:e + 1, :] if isinstance(e, int) else pb0s[:, bass.ds(e, 1), :]
                    v.tensor_tensor(ye[:, p, 0:4, :], bank[6][:, :].rearrange("p (k d) -> p k d", k=4),
                                    pbw.broadcast_to([P, 4, P]), ALU.add).then_inc(S["y_ready"], 1)
                    dve.wait_ge(S["dn_ps"], e * 2 + 2)
                    v.tensor_tensor(ye[:, p, 4, :], bank[7][:, 0:P], pe_, ALU.add).then_inc(S["y_ready"], 1)

                sweep(dve, E0, expert)
                for q in range(4):
                    dve.wait_ge(S[f"y_in{q}"], 32)
                    for k in range(2):
                        for b in range(4 * q, 4 * q + 4):
                            ge(dve, S["x2_ready"], (2 * q + k - 1) * 4 + b % 4 + 1 if k else 0)
                            v.scalar_tensor_tensor(xr[:, b, :], yt[:, k, b, :], wt0[:, k, b:b + 1], xr[:, b, :],
                                                   ALU.mult, ALU.add).then_inc(S["x2_ready"], 1)
                    for b in range(4 * q, 4 * q + 4):
                        dve.wait_ge(S["x2_ready"], 8 * q + 4 + b % 4 + 1)
                        v.bn_stats(st[:, b, :], xr[:, b, :]).then_inc(S["stats"], 1)
            if STOP >= 3:
                layer_norm(dve)
                attention_dve(dve, layers[1])
            if STOP >= 4:
                layer_norm(dve)
                for b in range(NB):
                    v.tensor_scalar(xn4[:, b, :], xr[:, b, :], mean[:, b:b + 1], rstd[:, b:b + 1],
                                    ALU.subtract, ALU.mult).then_inc(S["xn4_ready"], 1)
                dve.wait_ge(S["lg1_ps"], 1)
                lp = bank[2][:, 0:NB * E1].rearrange("p (b e) -> p b e", b=NB)
                link(dve, v.tensor_reduce(mx1[:, :], lp, AX, ALU.max, negate=True))
                v.tensor_tensor(sc1[:, :, :], lp, mx1[:, :].unsqueeze(2).broadcast_to([P, NB, E1]),
                                ALU.add).then_inc(S["sc1_in"], 1)
                dve.wait_ge(S["sc1_exp"], 1)
                link(dve, v.tensor_reduce(mx1[:, :], sc1[:, :, :], AX, ALU.add))
                link(dve, v.reciprocal(mx1[:, :], mx1[:, :]))
                v.tensor_tensor(sc1[:, :, :], sc1[:, :, :], mx1[:, :].unsqueeze(2).broadcast_to([P, NB, E1]),
                                ALU.mult).then_inc(S["sc1_ready"], 1)
                dve.wait_ge(S["st_sb"], 1)
                src, dst = sT, sT2
                for _ in range(CAP1 // 8):
                    for r in range(2):
                        link(dve, v.max(top8[:, r, :], src[:, r, :]))
                        link(dve, v.match_replace(dst[:, r, :], top8[:, r, :], src[:, r, :], -1.0))
                    src, dst = dst, src
                v.tensor_scalar(dst[:, :, :], src[:, :, :], -1.0, None, ALU.is_equal).then_inc(S["sel_ready"], 1)
                dve.wait_ge(S["se_ps"], 1)
                selp = bank[4][:, 0:2 * P].rearrange("p (b e) -> p b e", b=NB)
                link(dve, v.tensor_copy(sel1[:, :, :], selp))
                v.tensor_copy(sel1b[:, :, :], sel1[:, :, :]).then_inc(S["sel_rows"], 1)
                link(dve, v.tensor_tensor(w1t[:, :, :], sc1[:, :, :], sel1[:, :, :], ALU.mult))
                dve.wait_ge(S["pos_ps"], 1)
                posp = bank[5][:, 0:2 * P].rearrange("p (b e) -> p b e", b=NB)
                link(dve, v.scalar_tensor_tensor(pos1[:, :, :], posp, 1.0, sel1[:, :, :], ALU.add, ALU.mult))
                link(dve, v.tensor_scalar(pos1[:, :, :], pos1[:, :, :], -1.0, None, ALU.add))
                for b in range(NB):
                    v.tensor_tensor(hot1[:, b, :, :], pos1[:, b, :].unsqueeze(2).broadcast_to([P, E1, CAP1]),
                                    con[:, C_IOTA:C_IOTA + CAP1].unsqueeze(1).broadcast_to([P, E1, CAP1]),
                                    ALU.is_equal).then_inc(S["hot_ready"], 1)

                def gathered(b, p):
                    dve.wait_ge(S["gt_ps"], b + 1)
                    v.tensor_copy(xt1[:, :, b, :], bank[6 + p][:, 0:SLOTS1].rearrange("p (e c) -> p e c", e=E1)
                                  ).then_inc(S["gt_ready"], 1)
                sweep(dve, NB, gathered)

                def expert1(e, p):
                    dve.wait_ge(S["ge_ready"], e + 1)
                    ge(dve, S["eo_ps"], e - 1)
                    v.tensor_tensor(h1[:, p, :], g1[:, p, :], bank[2 + p][:, :], ALU.mult).then_inc(S["h_ready"], 1)
                    dve.wait_ge(S["eo_ps"], e + 1)
                    v.tensor_copy(eo1[:, :, e, :], bank[4 + p][:, 0:SLOTS1].rearrange("p (b c) -> p b c", b=NB)
                                  ).then_inc(S["eo_ready"], 1)
                sweep(dve, E1, expert1)

                dve.wait_ge(S["hot_ready"], NB)

                def weigh(b, p):
                    ge(dve, S["tt_ps"], b - 1)
                    wb = w1t[:, b:b + 1, :] if isinstance(b, int) else w1t[:, bass.ds(b, 1), :]
                    v.tensor_tensor(ows[:, p, :].rearrange("p (e c) -> p e c", e=E1), hot1[:, b, :, :],
                                    wb.rearrange("p o e -> p (o e)").unsqueeze(2).broadcast_to([P, E1, CAP1]),
                                    ALU.mult).then_inc(S["ow_ready"], 1)
                weigh(0, 0)

                def batch1(b, p):
                    if not is_last(b, NB):
                        weigh(b + 1, 1 - p)
                    dve.wait_ge(S["tt_ps"], b + 1)
                    ge(dve, S["fin_ps"], b - 1)
                    v.tensor_copy(owT[:, p, :, :], bank[p][:, 0:2 * P].rearrange("p (k d) -> p k d", k=2)
                                  ).then_inc(S["tt_ready"], 1)
                    dve.wait_ge(S["sg_ready"], b + 1)
                    v.tensor_tensor(hs[:, p, :], gs[:, p, :], bank[4 + p][:, F1:2 * F1], ALU.mult).then_inc(S["sh_ready"], 1)
                    dve.wait_ge(S["fin_ps"], b + 1)
                    ge(dve, S["out_odd" if p else "out_even"], (b - p) * 8)
                    v.scalar_tensor_tensor(yo[:, p, :], bank[6 + p][:, 0:P], gate_t[:, 3:4], xr[:, b, :],
                                           ALU.mult, ALU.add).then_inc(S["y_out_ready"], 1)
                sweep(dve, NB, batch1)

        @block.tensor
        def _(pe):
            def fold(h, p):
                pe.wait_ge(S["wkq_odd" if p else "wkq_even"], (h - p) * 8 + 16)
                ge(pe, S["m_ready"], h - 1)
                pe.matmul(bank[p][:, 0:P], wkq[:, p, 0, :], wkq[:, p, 1, :], start=True, stop=True).then_inc(S["m_ps"], 1)

            def keys(h, p):
                pe.wait_ge(S["m_ready"], h + 1)
                ge(pe, S["km_dve"], (h - 1) * 3)
                for c, (b0, nb) in enumerate(KM_CHUNKS):
                    pe.matmul(bank[2 + 3 * p + c][:, 0:nb * TK], m_sb[:, p, :], ctx_sb[:, b0 * TK:(b0 + nb) * TK],
                              start=True, stop=True).then_inc(S["km_ps"], 1)
            pe.wait_ge(S["ctx_in"], 16)
            fold(0, 0)

            def head(h, p):
                if not is_last(h, NH):
                    fold(h + 1, 1 - p)
                keys(h, p)
            sweep(pe, NH, head)
            pe.wait_ge(S["w0v_in"], 16)
            pe.wait_ge(S["km_dve"], 3 * NH)
            for b in range(NB):
                for hf in range(2):
                    n = 2 * b + hf
                    if n >= 8:
                        pe.wait_ge(S["v_act" if hf else "v_dve"], (n - 8) // 2 + 1)
                    pe.matmul(bank[n % 8][0:TK, :], ctx_sb[:, b * TK:(b + 1) * TK], wv0[:, hf * BANK:(hf + 1) * BANK],
                              start=True, stop=True).then_inc(S["v_ps"], 1)
            pe.wait_ge(S["v_act"], NB)
            pe.wait_ge(S["v_dve"], NB)
            pe.wait_ge(S["con_in"], 16)
            pe.wait_ge(S["w0o_in"], 16)
            attention_pe(pe, layers[0])

            if STOP >= 2:
                s0 = layers[0]["sem"]
                pe.wait_ge(S["small_in"], 16 * 5)
                pe.wait_ge(s0["sub_ready"], NB * NG)
                pe.wait_ge(s0["pT_ready"], NB * NG)
                for q in range(NB // 4):
                    pe.wait_ge(S["xn_ready"], 4 * q + 4)
                    ge(pe, S["xt_ready"], q - 1)
                    for r in range(4):
                        last = pe.transpose(bank[q % 2][:, P * r:P * r + P], xn[:, 4 * q + r, :], ident)
                    last.then_inc(S["xt_ps"], 1)
                for b in range(NB):
                    if b % 4 == 0:
                        pe.wait_ge(S["xt_ready"], b // 4 + 1)
                    last = pe.matmul(bank[2][:, b * E0:(b + 1) * E0], xnTa[:, b, :], gw0s[:, :], start=True, stop=True)
                last.then_inc(S["lg_ps"], 1)
                pe.wait_ge(S["w1_in"], 16 * 8)
                pe.wait_ge(s0["on_ready"], NB * NG)
                pe.wait_ge(s0["oT_ready"], 2 * NB)
                pe.wait_ge(s0["x_ready"], NB)
                for c, (b0, nb) in enumerate(KM_CHUNKS):
                    pe.matmul(bank[4 + c][:, 0:nb * TK], w1[:, 1, :], ctx_sb[:, b0 * TK:(b0 + nb) * TK],
                              start=True, stop=True).then_inc(S["k1_ps"], 1)
                pe.wait_ge(S["k1_act"], 3)
                for b in range(NB):
                    last = pe.matmul(bank[4 + b // 4][0:TK, P * (b % 4):P * (b % 4) + P],
                                     ctx_sb[:, b * TK:(b + 1) * TK], w1[:, 2, :], start=True, stop=True)
                    if b % 4 == 3:
                        last.then_inc(S["v1_ps"], 1)
                pe.wait_ge(S["consts_ready"], 1)
                pe.wait_ge(S["rank_in"], 2)
                rank = bank[3][:, 0:2 * NB * E0]
                pe.matmul(rank, tri[:, :], hotb[:, :, :].rearrange("p n e -> p (n e)"), start=True, stop=False)
                pe.matmul(rank, ones[:, :], cumb[:, :, :].rearrange("p n e -> p (n e)"), start=False,
                          stop=True).then_inc(S["rank_ps"], 1)
                pe.wait_ge(S["pos_ready"], 1)
                pe.wait_ge(S["lo_ready"], 1)
                pe.wait_ge(S["hi_ready"], 1)
                for n in range(2 * NB):
                    if n % 8 == 0:
                        pe.wait_ge(S["dve_pos"], n // 8 + 1)
                    last = pe.matmul(bank[2][:, BANK // 2:BANK // 2 + 2 * TILES0].rearrange("p (k n) -> p k n", k=2),
                                     at_pos[:, n, :], in_tile[:, 1:3, n, :],
                                     start=(n == 0), stop=(n == 2 * NB - 1))
                last.then_inc(S["id_ps"], 1)
                pe.wait_ge(S["v1_ready"], NB)

                def turn(e, p):
                    pe.wait_ge(S["xe_odd" if p else "xe_even"], (e - p) * (8 * ST0) + 16 * ST0)
                    ge(pe, S["t_ready"], e * 2)
                    for k in range(ST0):
                        last = pe.transpose(bank[k // 4][:, P * (k % 4):P * (k % 4) + P], xe[:, p, k, :], ident)
                    last.then_inc(S["t_ps"], 1)

                turn(0, 0)
                pe.wait_ge(S["put_ready"], 1)

                def expert(e, p):
                    pe.wait_ge(S["fe_odd" if p else "fe_even"], (e - p) * 24 + 48)
                    pe.wait_ge(S["t_ready"], e * 2 + 2)
                    for n in range(8):
                        c, w = n // 2, n % 2
                        if n >= 4:
                            pe.wait_ge(S["up_ready"], e * 8 + n - 3)
                        else:
                            ge(pe, S["up_ready"], e * 8 + n - 3)
                        pe.matmul(bank[2 + n % 4][:, 0:320], fc[:, p, P * c:P * c + P], xeT[:, p, 320 * w:320 * w + 320],
                                  start=True, stop=True).then_inc(S["up_ps"], 1)
                    if not is_last(e, E0):
                        turn(e + 1, 1 - p)
                    pe.wait_ge(S["up_ready"], e * 8 + 8)
                    for k in range(ST0):
                        if k == 0:
                            ge(pe, S["y_ready"], e * 2)
                        for c in range(F0 // P):
                            last = pe.matmul(bank[6 + k // 4][:, P * (k % 4):P * (k % 4) + P],
                                             hT[:, p, c, P * k:P * k + P], pj[:, p, c, :],
                                             start=(c == 0), stop=(c == F0 // P - 1))
                        if k >= 3:
                            last.then_inc(S["dn_ps"], 1)
                sweep(pe, E0, expert)
            if STOP >= 3:
                pe.wait_ge(S["y_ready"], 2 * E0)
                pe.wait_ge(S["mask_ready"], 1)
                attention_pe(pe, layers[1])
            if STOP >= 4:
                s1 = layers[1]["sem"]
                pe.wait_ge(s1["sub_ready"], NB * NG)
                pe.wait_ge(s1["pT_ready"], NB * NG)
                for q in range(NB // 4):
                    pe.wait_ge(S["xn4_ready"], 4 * q + 4)
                    ge(pe, S["x4_ready"], q - 1)
                    for r in range(4):
                        last = pe.transpose(bank[q % 2][:, P * r:P * r + P], xn4[:, 4 * q + r, :], ident)
                    last.then_inc(S["x4_ps"], 1)
                for b in range(NB):
                    if b % 4 == 0:
                        pe.wait_ge(S["x4_ready"], b // 4 + 1)
                    last = pe.matmul(bank[2][:, b * E1:(b + 1) * E1], xn4T[:, b, :], gw1s[:, :], start=True, stop=True)
                last.then_inc(S["lg1_ps"], 1)
                pe.wait_ge(S["sc1_ready"], 1)
                sc_rows = sc1[:, :, :].rearrange("p b e -> p (b e)")
                for r in range(2):
                    last = pe.transpose(bank[3][:, P * r:P * r + P], sc_rows[:, P * r:P * r + P], ident)
                last.then_inc(S["st_ps"], 1)
                pe.wait_ge(S["sel_ready"], 1)
                chosen = sT2 if (CAP1 // 8) % 2 == 0 else sT
                for r in range(2):
                    last = pe.transpose(bank[4][:, P * r:P * r + P], chosen[:, r, :], ident)
                last.then_inc(S["se_ps"], 1)
                pe.wait_ge(S["sel_rows"], 1)
                pe.matmul(bank[5][:, 0:2 * P], tri[:, :], sel1b[:, :, :].rearrange("p b e -> p (b e)"),
                          start=True, stop=True).then_inc(S["pos_ps"], 1)
                pe.wait_ge(S["hot_ready"], NB)

                def gather(b, p):
                    pe.wait_ge(S["xst_ready"], b + 1)
                    ge(pe, S["gt_ready"], b - 1)
                    pe.matmul(bank[6 + p][:, 0:SLOTS1], xs[:, p, :], hot1[:, b, :, :].rearrange("p e c -> p (e c)"),
                              start=True, stop=True).then_inc(S["gt_ps"], 1)
                sweep(pe, NB, gather)
                pe.wait_ge(S["gt_ready"], NB)

                def up(e, p):
                    pe.wait_ge(S["we_odd" if p else "we_even"], (e - p) * 24 + 48)
                    ge(pe, S["h_ready"], e - 1)
                    xe_ = xt1[:, e, :, :].rearrange("p b c -> p (b c)")
                    for k in range(2):
                        for c in range(F1 // P):
                            last = pe.matmul(bank[2 * k + p][:, SLOTS1 * c:SLOTS1 * (c + 1)],
                                             wgu[:, p, k, P * c:P * c + P], xe_, start=True, stop=True)
                    last.then_inc(S["gu_ps"], 1)

                def down(e, p):
                    pe.wait_ge(S["h_ready"], e + 1)
                    ge(pe, S["eo_ready"], e - 1)
                    for c in range(F1 // P):
                        last = pe.matmul(bank[4 + p][:, 0:SLOTS1], wdd[:, p, c, :], h1[:, p, SLOTS1 * c:SLOTS1 * (c + 1)],
                                         start=(c == 0), stop=(c == F1 // P - 1))
                    last.then_inc(S["eo_ps"], 1)
                up(0, 0)

                def expert1(e, p):
                    if not is_last(e, E1):
                        up(e + 1, 1 - p)
                    down(e, p)
                sweep(pe, E1, expert1)
                pe.wait_ge(S["eo_ready"], E1)

                def batch1(b, p):
                    ge(pe, S["sh_ready"], b - 1)
                    for k in range(2):
                        for c in range(F1 // P):
                            last = pe.matmul(bank[4 + p][:, F1 * k + P * c:F1 * k + P * c + P], wss[:, k, P * c:P * c + P],
                                             xn4T[:, b, :], start=True, stop=True)
                    last.then_inc(S["sgu_ps"], 1)
                    pe.wait_ge(S["ow_ready"], b + 1)
                    pe.wait_ge(S["es_ready"], b + 1)
                    ge(pe, S["tt_ready"], b - 1)
                    ge(pe, S["et_ready"], b - 1)
                    for r in range(2):
                        pe.transpose(bank[p][:, P * r:P * r + P], ows[:, p, P * r:P * r + P], ident)
                        last = pe.transpose(bank[2 + p][:, P * r:P * r + P], eos[:, p, P * r:P * r + P], ident)
                    last.then_inc(S["tt_ps"], 1)

                def combine(b, p):
                    pe.wait_ge(S["tt_ready"], b + 1)
                    pe.wait_ge(S["et_ready"], b + 1)
                    ge(pe, S["y_out_ready"], b - 1)
                    y = bank[6 + p][:, 0:P]
                    for r in range(2):
                        pe.matmul(y, owT[:, p, r, :], eoT[:, p, r, :], start=(r == 0), stop=False)
                    pe.wait_ge(S["sh_ready"], b + 1)
                    for c in range(F1 // P):
                        last = pe.matmul(y, hs[:, p, P * c:P * c + P], wss[:, 2, P * c:P * c + P], start=False,
                                         stop=(c == F1 // P - 1))
                    last.then_inc(S["fin_ps"], 1)
                batch1(0, 0)

                def turn1(b, p):
                    if not is_last(b, NB):
                        batch1(b + 1, 1 - p)
                    combine(b, p)
                sweep(pe, NB, turn1)


def kernel(**inputs):
    import concourse.bacc as bacc
    from concourse.bass_utils import run_bass_kernel_spmd

    a = {k: np.ascontiguousarray(v) for k, v in inputs.items()}
    c = np.ascontiguousarray
    arrays = dict(
        x=a["x"].reshape(NB * P, P),
        ctxT=c(a["ctx_1024"].reshape(NB * TK, P).T),
        maskb=a["mask_BxS2_bf1"].view(np.uint8).reshape(NB * TK),
        gates=np.concatenate([a["g_xattn"], a["g_ffn"]]),
        consts=constants(),
        w0kq=c(np.stack([a["L0_xattn_Wk"].transpose(1, 2, 0), a["L0_xattn_Wq"].transpose(1, 2, 0)], 2)),
        w0v=a["L0_xattn_Wv"].reshape(P, NH * D0),
        w0o=a["L0_xattn_Wo"].reshape(NH * D0, P),
        gw0=a["L0_ffn_gate_w"],
        fc0=a["L0_ffn_c_fc"],
        fb0=c(a["L0_ffn_fc_bias"].reshape(E0, F0 // P, P).transpose(0, 2, 1)),
        pj0=a["L0_ffn_c_proj"],
        pb0=a["L0_ffn_proj_bias"].reshape(E0, P),
        w1q=c(a["L1_xattn_Wq"].T), w1k=c(a["L1_xattn_Wk"].T), w1v=c(a["L1_xattn_Wv"].T), w1o=c(a["L1_xattn_Wo"].T),
        b1q=a["L1_xattn_bq"], b1k=a["L1_xattn_bk"], b1v=a["L1_xattn_bv"], b1o=a["L1_xattn_bo"],
        gw1=c(a["L1_ffn_gate_w"].T),
        wg1=c(a["L1_ffn_Wg"].transpose(0, 2, 1)), wu1=c(a["L1_ffn_Wu"].transpose(0, 2, 1)),
        wd1=c(a["L1_ffn_Wd"].transpose(0, 2, 1)),
        wsg=c(a["L1_ffn_Ws_g"].T), wsu=c(a["L1_ffn_Ws_u"].T), wsd=c(a["L1_ffn_Ws_d"].T),
    )
    nc = bacc.Bacc("TRN2", target_bir_lowering=False, num_devices=1)
    aps = {n: nc.dram_tensor(n, v.shape, mybir.dt.from_np(v.dtype), kind="ExternalInput").ap()
           for n, v in arrays.items()}
    aps["out"] = nc.dram_tensor("out", (NB * P, P), F32, kind="ExternalOutput").ap()
    program(nc, **aps)
    r = run_bass_kernel_spmd(nc, [arrays], core_ids=[0])
    return r.results[0]["out"].reshape(NB, P, P)
```
